# Optimizing a Trainium2 kernel written in Bass

```python
import numpy as np
import jax
import jax.numpy as jnp

def _softmax(x, axis=-1):
    return jax.nn.softmax(x, axis=axis)

def _gelu(x):
    return jax.nn.gelu(x, approximate=True)

def _silu(x):
    return jax.nn.silu(x)

def _sigmoid(x):
    return jax.nn.sigmoid(x)

def _layernorm(x, axis=-1, eps=1e-05):
    m = jnp.mean(x, axis=axis, keepdims=True)
    v = jnp.var(x, axis=axis, keepdims=True)
    return (x - m) / jnp.sqrt(v + eps)

def _scatter_add(tgt, idx, src, axis=0):
    return tgt.at[idx].add(src)

def _segment_sum(src, seg, n):
    return jax.ops.segment_sum(src, seg, n)
kernel_name = 'mk_gnn_resnorm_d2_gnn_r16_bc76da'

def setup_inputs(seed: int=0):
    np.random.seed(seed)
    _w = jnp.asarray

    def _rec_inputs():
        import jax
        import jax.numpy as jnp
        _gk = jax.random.key(seed)
        x = -0.0003713 + 1 * jax.random.normal(jax.random.fold_in(_gk, 1), (6250, 128), jnp.float32)
        _s = jax.random.randint(jax.random.fold_in(_gk, 2), (100000,), 0, 6250, jnp.int32)
        _d = jax.random.randint(jax.random.fold_in(_gk, 3), (100000,), 0, 6250, jnp.int32)
        _loop = jnp.arange(6250, dtype=jnp.int32)
        src = jnp.concatenate([_s, _d, _loop])
        dst = jnp.concatenate([_d, _s, _loop])
        _o = jnp.argsort(dst, stable=True)
        src = src[_o]
        dst = dst[_o]
        edge_attr_16 = 0.000254156 + 0.999948 * jax.random.normal(jax.random.fold_in(_gk, 11), (206250, 16), jnp.float32)
        edge_attr_16_n2 = 0.000254156 + 0.999948 * jax.random.normal(jax.random.fold_in(_gk, 12), (206250, 16), jnp.float32)
        return (x, src, dst, edge_attr_16, edge_attr_16_n2)
    x, src, dst, edge_attr_16, edge_attr_16_n2 = _rec_inputs()

    def _L0_gnn_setup():
        import jax, jax.numpy as jnp
        import numpy as np
        N_NODES = 6250
        N_EDGES = 100000
        D = 128
        K = 5
        ALPHA = 0.1
        key = jax.random.key(seed)
        k1, k2, k3 = jax.random.split(key, 3)
        x = jax.random.normal(k1, (N_NODES, D), dtype=jnp.float32)
        edge_index = jax.random.randint(k2, (2, N_EDGES), 0, N_NODES, dtype=jnp.int64)
        weight = jax.random.normal(k3, (D, D), dtype=jnp.float32) * (1.0 / np.sqrt(D))
        bias = jnp.zeros((D,), dtype=jnp.float32)
        return {'x': x, 'edge_index': edge_index, 'weight': weight, 'bias': bias}
    _L0_gnn_all = _L0_gnn_setup()
    _L0_gnn_in = {k: v for k, v in _L0_gnn_all.items() if k in ('weight', 'bias')}
    del _L0_gnn_all

    def _L1_gnn_setup():
        import jax, jax.numpy as jnp
        import numpy as np
        N = 3125
        E = 50000
        D_IN = 128
        SH = 16
        EA = 16
        H = 8
        DQ = 64
        DK = 64
        DV = 128
        HID = 64

        def _conv_per_edge(x_src, edge_attr, edge_sh, Wang, Wlin, W1, b1, W2):
            rad = jax.nn.relu(edge_attr @ W1 + b1) @ W2
            g = edge_sh @ Wang.T
            return x_src * g @ Wlin * rad
        key = jax.random.key(seed)
        ks = jax.random.split(key, 20)
        g = lambda k, shape, fan: jax.random.normal(k, shape, jnp.float32) / np.sqrt(fan)
        return {'node_attr': jax.random.normal(ks[0], (N, D_IN), jnp.float32), 'edge_attr': jax.random.normal(ks[1], (E, EA), jnp.float32), 'edge_sh': jax.random.normal(ks[2], (E, SH), jnp.float32), 'Wq': g(ks[3], (D_IN, DQ), D_IN), 'Wang_k': g(ks[4], (D_IN, SH), SH), 'Wlin_k': g(ks[5], (D_IN, DK), D_IN), 'W1k': g(ks[6], (EA, HID), EA), 'b1k': jnp.zeros((HID,), jnp.float32), 'W2k': g(ks[7], (HID, DK), HID), 'Wang_v': g(ks[8], (D_IN, SH), SH), 'Wlin_v': g(ks[9], (D_IN, DV), D_IN), 'W1v': g(ks[10], (EA, HID), EA), 'b1v': jnp.zeros((HID,), jnp.float32), 'W2v': g(ks[11], (HID, DV), HID), 'Wdot': g(ks[12], (DQ // H, DK // H), DQ // H), 'Wout': g(ks[13], (DV, DV), DV), 'edge_index': jax.random.randint(ks[14], (2, E), 0, N, jnp.int64)}
    _L1_gnn_all = _L1_gnn_setup()
    _L1_gnn_in = {k: v for k, v in _L1_gnn_all.items() if k in ('Wq', 'Wang_k', 'Wlin_k', 'W1k', 'b1k', 'W2k', 'Wang_v', 'Wlin_v', 'W1v', 'b1v', 'W2v', 'Wdot', 'Wout')}
    del _L1_gnn_all
    return {'x': x, 'src': src, 'dst': dst, 'edge_attr_16': edge_attr_16, 'edge_attr_16_n2': edge_attr_16_n2, 'L0_gnn_weight': _L0_gnn_in['weight'], 'L0_gnn_bias': _L0_gnn_in['bias'], 'L1_gnn_Wq': _L1_gnn_in['Wq'], 'L1_gnn_Wang_k': _L1_gnn_in['Wang_k'], 'L1_gnn_Wlin_k': _L1_gnn_in['Wlin_k'], 'L1_gnn_W1k': _L1_gnn_in['W1k'], 'L1_gnn_b1k': _L1_gnn_in['b1k'], 'L1_gnn_W2k': _L1_gnn_in['W2k'], 'L1_gnn_Wang_v': _L1_gnn_in['Wang_v'], 'L1_gnn_Wlin_v': _L1_gnn_in['Wlin_v'], 'L1_gnn_W1v': _L1_gnn_in['W1v'], 'L1_gnn_b1v': _L1_gnn_in['b1v'], 'L1_gnn_W2v': _L1_gnn_in['W2v'], 'L1_gnn_Wdot': _L1_gnn_in['Wdot'], 'L1_gnn_Wout': _L1_gnn_in['Wout']}

def reference(x, src, dst, edge_attr_16, edge_attr_16_n2, L0_gnn_weight, L0_gnn_bias, L1_gnn_Wq, L1_gnn_Wang_k, L1_gnn_Wlin_k, L1_gnn_W1k, L1_gnn_b1k, L1_gnn_W2k, L1_gnn_Wang_v, L1_gnn_Wlin_v, L1_gnn_W1v, L1_gnn_b1v, L1_gnn_W2v, L1_gnn_Wdot, L1_gnn_Wout):
    import jax
    import jax.numpy as jnp

    def _L0_gnn_ref(x, edge_index, weight, bias):
        import jax, jax.numpy as jnp
        import numpy as np
        N_NODES = 6250
        N_EDGES = 100000
        D = 128
        K = 5
        ALPHA = 0.1
        N = x.shape[0]
        loops = jnp.tile(jnp.arange(N, dtype=edge_index.dtype)[None, :], (2, 1))
        ei = jnp.concatenate([edge_index, loops], axis=1)
        ew = jnp.ones((ei.shape[1],), dtype=x.dtype)
        row, col = (ei[0], ei[1])
        deg = jax.ops.segment_sum(ew, col, num_segments=N)
        dinv = jnp.where(deg > 0, jax.lax.rsqrt(deg), 0.0).astype(x.dtype)
        w = dinv[row] * ew * dinv[col]

        def spmm(h):
            return jax.ops.segment_sum(h[col] * w[:, None], row, num_segments=N)
        x_out = x * ALPHA
        h = x
        coef = (1.0 - ALPHA) / K
        for _ in range(K):
            h = spmm(h)
            x_out = x_out + coef * h
        return x_out @ weight.T + bias

    def _L1_gnn_ref(node_attr, edge_attr, edge_sh, Wq, Wang_k, Wlin_k, W1k, b1k, W2k, Wang_v, Wlin_v, W1v, b1v, W2v, Wdot, Wout, edge_index):
        import jax, jax.numpy as jnp
        import numpy as np
        N = 3125
        E = 50000
        D_IN = 128
        SH = 16
        EA = 16
        H = 8
        DQ = 64
        DK = 64
        DV = 128
        HID = 64

        def _conv_per_edge(x_src, edge_attr, edge_sh, Wang, Wlin, W1, b1, W2):
            rad = jax.nn.relu(edge_attr @ W1 + b1) @ W2
            g = edge_sh @ Wang.T
            return x_src * g @ Wlin * rad
        src, dst = (edge_index[0], edge_index[1])
        n = node_attr.shape[0]
        e = src.shape[0]
        q = (node_attr @ Wq).reshape(n, H, DQ // H)
        x_src = node_attr[src]
        k = _conv_per_edge(x_src, edge_attr, edge_sh, Wang_k, Wlin_k, W1k, b1k, W2k).reshape(e, H, DK // H)
        v = _conv_per_edge(x_src, edge_attr, edge_sh, Wang_v, Wlin_v, W1v, b1v, W2v).reshape(e, H, DV // H)
        alpha = jnp.einsum('ehq,qk,ehk->eh', q[dst], Wdot, k)
        amax = jax.ops.segment_max(alpha, dst, num_segments=n)
        ealpha = jnp.exp(alpha - amax[dst])
        denom = jax.ops.segment_sum(ealpha, dst, num_segments=n)
        attn = ealpha / denom[dst]
        out = jax.ops.segment_sum(attn[..., None] * v, dst, num_segments=n)
        return out.reshape(n, DV) @ Wout
    edge_index = jnp.stack([src, dst])
    x = _layernorm(x + _L0_gnn_ref(x, edge_index, L0_gnn_weight, L0_gnn_bias), axis=-1)
    x = _layernorm(x + _L1_gnn_ref(x, edge_attr_16, edge_attr_16_n2, L1_gnn_Wq, L1_gnn_Wang_k, L1_gnn_Wlin_k, L1_gnn_W1k, L1_gnn_b1k, L1_gnn_W2k, L1_gnn_Wang_v, L1_gnn_Wlin_v, L1_gnn_W1v, L1_gnn_b1v, L1_gnn_W2v, L1_gnn_Wdot, L1_gnn_Wout, edge_index), axis=-1)
    return x

_drawn_inputs = setup_inputs


def setup_inputs(seed=0):
    import zlib

    import numpy as np

    out = dict(_drawn_inputs(seed))
    spreads = {'L0_gnn_bias': (0.0, 0.1), 'L1_gnn_b1k': (0.0, 0.1), 'L1_gnn_b1v': (0.0, 0.1)}
    factors = {}
    for name, (base, spread) in spreads.items():
        noise = np.random.default_rng([zlib.crc32(name.encode()), seed]).standard_normal(out[name].shape)
        drawn = base * np.exp(spread * noise) if base else spread * noise
        out[name] = jnp.asarray(drawn.astype(out[name].dtype))
    for name, factor in factors.items():
        out[name] = (out[name] * factor).astype(out[name].dtype)
    return out
```

```python
from contextlib import ExitStack

import numpy as np

import concourse.bass as bass
from concourse import mybir

F32 = mybir.dt.float32
BF16 = mybir.dt.bfloat16
I32 = mybir.dt.int32
ALU = mybir.AluOpType
ACT = mybir.ActivationFunctionType
AX = mybir.AxisListType

P = 128
D = 128
DQ = 64
H = 8
EA = 16
HID = 64
GT = 4
GE = GT * P
HOPS = 5
ALPHA = 0.1
EPS = 1e-5
BIG = 1.0e30
ROW = D + H
MARK = 4096.0


def first(k):
    return isinstance(k, int) and k == 0


def in_pairs(eng, step, n):
    step(0, 0)
    step(0, 1)
    if n > 1:
        with eng.Fori(1, n) as k:
            step(k, 0)
            step(k, 1)


def program(nc, a, out):
    N = a["n_nodes"]
    NB = a["x"].shape[0] // P
    NP = NB * P
    TILES = a["src_cols"].shape[1]
    G = TILES // GT
    TRASH = NP * NB
    halves = [(0, (NB + 1) // 2), ((NB + 1) // 2, NB)]

    T_flat = nc.dram_tensor("adjacency", [(TRASH + GE) * P, 1], F32, kind="Internal").ap()
    T = T_flat[0:NP * NP, :].rearrange("(d s) o -> d (s o)", s=NP)
    x1_table = nc.dram_tensor("x1_table", [NP, D], F32, kind="Internal").ap()
    q_table = nc.dram_tensor("q_table", [NP, DQ], F32, kind="Internal").ap()
    sums_table = nc.dram_tensor("sums_table", [G * GE, ROW], F32, kind="Internal").ap()

    def by_block(t):
        return t.rearrange("(b p) d -> p b d", p=P)

    with ExitStack() as whole:
        def keep(name, shape, dt=F32):
            return whole.enter_context(nc.sbuf_tensor(name, shape, dt))

        ident = keep("ident", [P, P])
        dinv = keep("dinv", [P, NB])
        last_edge = keep("last_edge", [P, NB], I32)
        has_edges = keep("has_edges", [P, NB])
        x_res = keep("x_res", [P, NB, D])
        feats = keep("feats", [P, NB, D])

        build_adjacency(nc, a, T_flat, T, ident, dinv, last_edge, has_edges, NB, NP, G, TRASH)
        propagate(nc, a, T, ident, dinv, x_res, feats, by_block, NB, halves)
        node_layer(nc, "l0", NB, N, ident, x_res, feats, a["w0_t"], a["b0"],
                   by_block(x1_table), a, by_block(q_table))
        edge_attention(nc, a, x1_table, q_table, sums_table, ident, G)
        attention_output(nc, sums_table, last_edge, has_edges, feats, NB)
        node_layer(nc, "l1", NB, N, ident, x_res, feats, a["Wout"], None, out, None, None)


def build_adjacency(nc, a, T_flat, T, ident, dinv, last_edge, has_edges, NB, NP, G, TRASH):
    TILES = G * GT
    with ExitStack() as ctx:
        def sb(name, shape, dt=F32):
            return ctx.enter_context(nc.sbuf_tensor(name, shape, dt))

        def sem(name):
            return ctx.enter_context(nc.semaphore(name))

        src_i = sb("src_i", [P, TILES], I32)
        dst_i = sb("dst_i", [P, TILES], I32)
        low_i = sb("low_i", [P, TILES], I32)
        tmp_i = sb("tmp_i", [P, TILES], I32)
        src_f = sb("src_f", [P, TILES])
        dst_f = sb("dst_f", [P, TILES])
        high_f = sb("high_f", [P, TILES])
        dlo_f = sb("dlo_f", [P, TILES])
        dhi_f = sb("dhi_f", [P, TILES])
        zeros = sb("zeros", [P, NP])
        order = sb("order", [P, GT, GE])
        iota_i = sb("iota_i", [P, P], I32)
        iota_f = sb("iota_f", [P, P])
        trash = sb("trash", [P, GT])
        trash_i = sb("trash_i", [P, GT], I32)
        ones = sb("ones", [P, P])
        pause = sb("pause", [1, 1])
        upper = sb("upper", [P, P])
        src_row = [sb(f"src_row{s}", [P, GE], I32) for s in range(2)]
        dst_row = [sb(f"dst_row{s}", [P, GE], I32) for s in range(2)]
        same_dst = [sb(f"same_dst{j}", [P, GE]) for j in range(GT)]
        total = [sb(f"total{s}", [P, GT]) for s in range(2)]
        gap = [sb(f"gap{s}", [P, GT]) for s in range(2)]
        move = [sb(f"move{s}", [P, GT]) for s in range(2)]
        place = [sb(f"place{s}", [P, GT], I32) for s in range(2)]
        address = [sb(f"address{s}", [P, GT], I32) for s in range(2)]
        one_lo = [sb(f"one_lo{s}", [P, GT, P], BF16) for s in range(2)]
        one_hi = [sb(f"one_hi{s}", [P, GT, NB], BF16) for s in range(2)]
        zero_bf = sb("zero_bf", [P, P], BF16)
        deg = sb("deg", [P, NB])
        count = sb("count", [P, NB])
        before = sb("before", [P, NB])
        root = sb("root", [P, NB])
        upto = sb("upto", [P, NB])
        scan_one = sb("scan_one", [P, NB])
        deg_ps = ctx.enter_context(nc.psum_tensor("deg_ps", [P, 512], F32))
        pre_ps = ctx.enter_context(nc.psum_tensor("pre_ps", [P, 512], F32))
        col_ps = ctx.enter_context(nc.psum_tensor("col_ps", [P, 512], F32))

        cols_in = sem("cols_in")
        pool_const = sem("pool_const")
        pool_step = sem("pool_step")
        paused = sem("paused")
        dve_prep = sem("dve_prep")
        zeros_set = sem("zeros_set")
        cleared = sem("cleared")
        row_in = [sem("row_in0"), sem("row_in1")]
        marked = sem("marked")
        counted = sem("counted")
        small = sem("small")
        ready = sem("ready")
        landed = sem("landed")
        onehot = sem("onehot")
        onehot_used = sem("onehot_used")
        deg_done = sem("deg_done")
        fin = sem("fin")
        rooted = sem("rooted")
        prefixed = sem("prefixed")
        block = ctx.enter_context(nc.Block())

        @block.sync
        def _(sp):
            sp.dma_start(src_i[:], a["src_cols"]).then_inc(cols_in, 16)
            sp.dma_start(dst_i[:], a["dst_cols"]).then_inc(cols_in, 16)

            def load_rows(k, s):
                g = k * 2 + s
                if not first(k):
                    sp.wait_ge(counted, GT * g - GT)
                lo = bass.ds(g * GE, GE)
                sp.dma_start(src_row[s][:], a["src"][:, lo].to_broadcast([P, GE])).then_inc(row_in[s], 16)
                sp.dma_start(dst_row[s][:], a["dst"][:, lo].to_broadcast([P, GE])).then_inc(row_in[s], 16)

            in_pairs(sp, load_rows, G // 2)

        @block.scalar
        def _(act):
            act.wait_ge(zeros_set, 1)
            for b in range(NB):
                act.dma_start(T[b * P:(b + 1) * P, :], zeros[:]).then_inc(cleared, 16)
            tail = GE // P
            for t in range(tail):
                lo = (TRASH + t * P) * P
                act.dma_start(T_flat[lo:lo + P * P, :].rearrange("(p c) o -> p (c o)", p=P),
                              zeros[:, 0:P]).then_inc(cleared, 16)
            act.wait_ge(fin, 2)
            nc.scalar.activation(root[:], deg[:], ACT.Sqrt).then_inc(rooted, 1)

        @block.gpsimd
        def _(pool):
            nc.gpsimd.memset(zeros[:], 0.0).then_inc(zeros_set, 1)
            nc.gpsimd.memset(ones[:], 1.0).then_inc(pool_step, 1)
            nc.gpsimd.memset(pause[:], 0.0).then_inc(pool_step, 1)
            nc.gpsimd.memset(order[:], 1.0).then_inc(pool_step, 1)
            nc.gpsimd.iota(iota_i[:], [[1, P]], base=0, channel_multiplier=0).then_inc(pool_const, 1)
            nc.gpsimd.iota(trash_i[:], [[P, GT]], base=0, channel_multiplier=1).then_inc(pool_const, 1)
            pool.wait_ge(pool_step, 3)
            nc.gpsimd.affine_select(out=ident[:], in_=ones[:], compare_op=ALU.is_equal, fill=0.0, base=0,
                                    pattern=[[1, P]], channel_multiplier=-1).then_inc(pool_const, 1)
            nc.gpsimd.affine_select(out=upper[:], in_=ones[:], compare_op=ALU.is_ge, fill=0.0, base=0,
                                    pattern=[[1, P]], channel_multiplier=-1).then_inc(pool_const, 1)
            for j in range(GT):
                nc.gpsimd.affine_select(out=order[:, j, :], in_=order[:, j, :], compare_op=ALU.is_ge,
                                        fill=1.0 + MARK, base=-P * j, pattern=[[1, GE]],
                                        channel_multiplier=-1).then_inc(pool_const, 1)

            def add_group(k, s):
                g = k * 2 + s
                pool.wait_ge(ready, g + 1)
                if not (first(k) and s == 0):
                    pool.wait_ge(landed, 64 * g)
                    pool.wait_ge(paused, g)
                nc.gpsimd.tensor_tensor(pause[:], pause[:], pause[:], ALU.add).then_inc(paused, 1)
                for j in range(GT):
                    nc.gpsimd.indirect_dma_start(
                        T_flat, bass.IndirectOffsetOnAxis(ap=address[s][:, j:j + 1], axis=0),
                        total[s][:, j:j + 1], None, compute_op=ALU.add).then_inc(landed, 16)

            pool.wait_ge(cleared, 16 * (NB + GE // P))
            in_pairs(pool, add_group, G // 2)
            pool.wait_ge(landed, 64 * G)

        @block.vector
        def _(dve):
            n_small = [0]

            def chain(ins):
                n_small[0] += 1
                ins.then_inc(dve_prep, 1)
                dve.wait_ge(dve_prep, n_small[0])

            dve.wait_ge(pool_const, 4 + GT)
            dve.wait_ge(cols_in, 32)
            nc.vector.memset(zero_bf[:], 0.0).then_inc(onehot, 1)
            nc.vector.memset(scan_one[:], 1.0)
            nc.vector.tensor_copy(iota_f[:], iota_i[:])
            chain(nc.vector.tensor_copy(trash[:], trash_i[:]))
            nc.vector.tensor_copy(src_f[:], src_i[:])
            nc.vector.tensor_copy(dst_f[:], dst_i[:])
            chain(nc.vector.tensor_scalar(trash[:], trash[:], float(TRASH), None, ALU.add))
            nc.vector.tensor_scalar(low_i[:], src_i[:], P - 1, None, ALU.bitwise_and)
            chain(nc.vector.tensor_scalar(tmp_i[:], src_i[:], 7, None, ALU.logical_shift_right))
            chain(nc.vector.scalar_tensor_tensor(out=high_f[:], in0=dst_f[:], scalar=float(NB), in1=tmp_i[:],
                                                 op0=ALU.mult, op1=ALU.add))
            chain(nc.vector.tensor_scalar(tmp_i[:], dst_i[:], P - 1, None, ALU.bitwise_and))
            chain(nc.vector.tensor_copy(dlo_f[:], tmp_i[:]))
            chain(nc.vector.tensor_scalar(tmp_i[:], dst_i[:], 7, None, ALU.logical_shift_right))
            chain(nc.vector.tensor_copy(dhi_f[:], tmp_i[:]))

            def compare_group(k, s):
                g = k * 2 + s
                dve.wait_ge(row_in[s], 32 * k + 32)
                if not (first(k) and s == 0):
                    dve.wait_ge(counted, g * GT)
                for j in range(GT):
                    c = bass.ds(g * GT + j, 1)
                    nc.vector.scalar_tensor_tensor(
                        out=same_dst[j][:], in0=dst_row[s][:], scalar=dst_f[:, c], in1=order[:, j, :],
                        op0=ALU.is_equal, op1=ALU.mult).then_inc(marked, 1)
                if not first(k):
                    dve.wait_ge(landed, 64 * g - 64)
                for j in range(GT):
                    c = bass.ds(g * GT + j, 1)
                    dve.wait_ge(marked, g * GT + j + 1)
                    nc.vector.scalar_tensor_tensor(
                        out=same_dst[j][:], in0=src_row[s][:], scalar=src_f[:, c], in1=same_dst[j][:],
                        op0=ALU.is_equal, op1=ALU.mult,
                        accum_out=total[s][:, j:j + 1]).then_inc(counted, 1)
                c4 = bass.ds(g * GT, GT)
                if not first(k):
                    dve.wait_ge(onehot_used, g - 1)
                nc.vector.tensor_tensor(
                    one_lo[s][:], iota_f[:].unsqueeze(1).to_broadcast([P, GT, P]),
                    dlo_f[:, c4].unsqueeze(2).to_broadcast([P, GT, P]), ALU.is_equal)
                nc.vector.tensor_tensor(
                    one_hi[s][:], iota_f[:, 0:NB].unsqueeze(1).to_broadcast([P, GT, NB]),
                    dhi_f[:, c4].unsqueeze(2).to_broadcast([P, GT, NB]), ALU.is_equal).then_inc(onehot, 1)
                nc.vector.tensor_tensor(gap[s][:], high_f[:, c4], trash[:], ALU.subtract).then_inc(small, 1)
                dve.wait_ge(small, g * 3 + 1)
                dve.wait_ge(counted, g * GT + GT)
                nc.vector.scalar_tensor_tensor(out=move[s][:], in0=total[s][:], scalar=MARK, in1=gap[s][:],
                                               op0=ALU.is_ge, op1=ALU.mult).then_inc(small, 1)
                dve.wait_ge(small, g * 3 + 2)
                nc.vector.tensor_tensor(place[s][:], high_f[:, c4], move[s][:], ALU.subtract).then_inc(small, 1)
                dve.wait_ge(small, g * 3 + 3)
                nc.vector.scalar_tensor_tensor(out=address[s][:], in0=place[s][:], scalar=7, in1=low_i[:, c4],
                                               op0=ALU.logical_shift_left, op1=ALU.bitwise_or).then_inc(ready, 1)

            in_pairs(dve, compare_group, G // 2)
            dve.wait_ge(deg_done, 1)
            nc.vector.tensor_copy(count[:], deg_ps[:, 0:NB]).then_inc(fin, 1)
            nc.vector.tensor_scalar(deg[:], deg_ps[:, 0:NB], 1.0, None, ALU.add).then_inc(fin, 1)
            chain(nc.vector.tensor_scalar(has_edges[:], deg_ps[:, 0:NB], 1.0, None, ALU.is_ge))
            dve.wait_ge(prefixed, 1)
            chain(nc.vector.tensor_tensor_scan(out=upto[:], data0=scan_one[:], data1=col_ps[:, 0:NB],
                                               initial=0.0, op0=ALU.mult, op1=ALU.add))
            chain(nc.vector.tensor_tensor(before[:], upto[:], col_ps[:, 0:NB], ALU.subtract))
            chain(nc.vector.scalar_tensor_tensor(out=upto[:], in0=pre_ps[:, 0:NB], scalar=-1.0, in1=before[:],
                                                 op0=ALU.add, op1=ALU.add))
            chain(nc.vector.tensor_scalar(last_edge[:], upto[:], 0.0, None, ALU.max))
            dve.wait_ge(rooted, 1)
            nc.vector.reciprocal(dinv[:], root[:]).then_inc(dve_prep, 1)
            dve.wait_ge(dve_prep, n_small[0] + 1)

        @block.tensor
        def _(pe):
            pe.wait_ge(onehot, 1)
            nc.tensor.matmul(deg_ps[:, 0:NB], zero_bf[:], zero_bf[:, 0:NB], start=True, stop=False,
                             skip_group_check=True)

            def histogram(k, s):
                pe.wait_ge(onehot, k * 2 + s + 2)
                for j in range(GT):
                    mm = nc.tensor.matmul(deg_ps[:, 0:NB], one_lo[s][:, j, :], one_hi[s][:, j, :],
                                          start=False, stop=False, skip_group_check=True)
                mm.then_inc(onehot_used, 1)

            in_pairs(pe, histogram, G // 2)
            nc.tensor.matmul(deg_ps[:, 0:NB], zero_bf[:], zero_bf[:, 0:NB], start=False, stop=True,
                             skip_group_check=True).then_inc(deg_done, 1)
            pe.wait_ge(fin, 1)
            pe.wait_ge(pool_const, 4)
            nc.tensor.matmul(pre_ps[:, 0:NB], upper[:], count[:], start=True, stop=True)
            nc.tensor.matmul(col_ps[:, 0:NB], ones[:], count[:], start=True, stop=True).then_inc(prefixed, 1)


def propagate(nc, a, T, ident, dinv, x_res, feats, by_block, NB, halves):
    STEPS = 2 * NB
    RING = max(r for r in range(1, 8) if STEPS % r == 0)
    TURNS = STEPS // RING
    WIDE = max(b1 - b0 for b0, b1 in halves) * P
    chunks = [[(c, min(512, (b1 - b0) * P - c)) for c in range(0, (b1 - b0) * P, 512)] for b0, b1 in halves]
    on_act = [len(cs[0::2]) for cs in chunks]
    on_dve = [len(cs[1::2]) for cs in chunks]
    quads = [(b, min(4, NB - b)) for b in range(0, NB, 4)]
    NQ = len(quads)
    with ExitStack() as ctx:
        def sb(name, shape, dt=F32):
            return ctx.enter_context(nc.sbuf_tensor(name, shape, dt))

        def sem(name):
            return ctx.enter_context(nc.semaphore(name))

        ring = [sb(f"t_ring{r}", [P, WIDE]) for r in range(RING)]
        U = sb("scaled", [P, NB, D])
        HT = sb("summed_t", [D, NB * P])
        S1 = [sb(f"with_loop{s}", [P, 4, D]) for s in range(2)]
        dinv2 = sb("dinv2", [P, NB])
        acc = [ctx.enter_context(nc.psum_tensor(f"acc{c}", [P, 512], F32)) for c in range(7)]
        spare = ctx.enter_context(nc.psum_tensor("spare", [P, 512], F32))
        turned = [spare, acc[6]]

        x_in = sem("x_in")
        prep = sem("prep")
        t_in = [sem(f"t_in{r}") for r in range(RING)]
        t_used = sem("t_used")
        u_ready = sem("u_ready")
        acc_done = sem("acc_done")
        by_act = sem("by_act")
        by_dve = sem("by_dve")
        turn_done = sem("turn_done")
        looped = sem("looped")
        s1_added = sem("s1_added")
        cleared = sem("feats_cleared")
        final = sem("final")
        block = ctx.enter_context(nc.Block())

        def in_hops(eng, hop):
            hop(0)
            with eng.Fori(1, HOPS) as k:
                hop(k)

        @block.sync
        def _(sp):
            sp.dma_start(x_res[:], by_block(a["x"])).then_inc(x_in, 16)

            def hop(k):
                for m in range(STEPS):
                    half, b = divmod(m, NB)
                    b0, b1 = halves[half]
                    if m >= RING or not first(k):
                        sp.wait_ge(t_used, k * STEPS + m - RING + 1)
                    sp.dma_start(ring[m % RING][:, 0:(b1 - b0) * P],
                                 T[b * P:(b + 1) * P, b0 * P:b1 * P]).then_inc(t_in[m % RING], 16)

            in_hops(sp, hop)

        @block.tensor
        def _(pe):
            def hop(k):
                pe.wait_ge(u_ready, k + 1)
                for half in range(2):
                    if half == 1 or not first(k):
                        pe.wait_ge(by_act, k * sum(on_act) + (on_act[0] if half else 0))
                        if (half and on_dve[0]) or (not half and sum(on_dve)):
                            pe.wait_ge(by_dve, k * sum(on_dve) + (on_dve[0] if half else 0))
                    for b in range(NB):
                        m = half * NB + b
                        pe.wait_ge(t_in[m % RING], 16 * (k * TURNS + m // RING + 1))
                        for c, (lo, n) in enumerate(chunks[half]):
                            mm = nc.tensor.matmul(acc[c][:, 0:n], U[:, b, :], ring[m % RING][:, lo:lo + n],
                                                  start=(b == 0), stop=(b == NB - 1))
                            if b == NB - 1 and c < len(chunks[half]) - 1:
                                mm.then_inc(acc_done, 1)
                        mm.then_inc(t_used, 1)
                pe.wait_ge(by_act, (k + 1) * sum(on_act))
                if sum(on_dve):
                    pe.wait_ge(by_dve, (k + 1) * sum(on_dve))
                for q, (b, n) in enumerate(quads):
                    if q >= 2 or not first(k):
                        pe.wait_ge(looped, k * NQ + max(q - 1, 0))
                    for j in range(n):
                        tr = nc.tensor.transpose(turned[q % 2][:, j * P:(j + 1) * P],
                                                 HT[:, (b + j) * P:(b + j + 1) * P], ident[:])
                    tr.then_inc(turn_done, 1)

            in_hops(pe, hop)

        def chunk_ready(eng, k, half, c):
            before = sum(len(cs) - 1 for cs in chunks[:half])
            if c < len(chunks[half]) - 1:
                eng.wait_ge(acc_done, k * sum(len(cs) - 1 for cs in chunks) + before + c + 1)
            else:
                eng.wait_ge(t_used, k * STEPS + (half + 1) * NB)

        @block.scalar
        def _(act):
            def hop(k):
                for half in range(2):
                    for c, (lo, n) in enumerate(chunks[half]):
                        if c % 2 == 0:
                            chunk_ready(act, k, half, c)
                            at = halves[half][0] * P + lo
                            nc.scalar.copy(HT[:, at:at + n], acc[c][:, 0:n]).then_inc(by_act, 1)

            in_hops(act, hop)

        @block.gpsimd
        def _(pool):
            nc.gpsimd.memset(feats[:], 0.0).then_inc(cleared, 1)
            pool.wait_ge(cleared, 1)

            def hop(k):
                for q, (b, n) in enumerate(quads):
                    pool.wait_ge(looped, k * NQ + q + 1)
                    nc.gpsimd.tensor_tensor(feats[:, b:b + n, :], feats[:, b:b + n, :], S1[q % 2][:, 0:n, :],
                                            ALU.add).then_inc(s1_added, 1)

            in_hops(pool, hop)

        @block.vector
        def _(dve):
            dve.wait_ge(x_in, 16)
            nc.vector.tensor_tensor(dinv2[:], dinv[:], dinv[:], ALU.mult).then_inc(prep, 1)
            nc.vector.tensor_tensor(U[:], x_res[:], dinv[:].unsqueeze(2).to_broadcast([P, NB, D]),
                                    ALU.mult).then_inc(u_ready, 1)
            dve.wait_ge(prep, 1)

            def hop(k):
                for half in range(2):
                    for c, (lo, n) in enumerate(chunks[half]):
                        if c % 2 == 1:
                            chunk_ready(dve, k, half, c)
                            at = halves[half][0] * P + lo
                            nc.vector.tensor_copy(HT[:, at:at + n], acc[c][:, 0:n]).then_inc(by_dve, 1)
                for q, (b, n) in enumerate(quads):
                    dve.wait_ge(turn_done, k * NQ + q + 1)
                    if q == 0:
                        dve.wait_ge(u_ready, k + 1)
                    if q >= 2 or not first(k):
                        dve.wait_ge(s1_added, k * NQ + max(q - 1, 0))
                    nc.vector.tensor_tensor(S1[q % 2][:, 0:n, :],
                                            turned[q % 2][:, 0:n * P].rearrange("p (b d) -> p b d", d=D),
                                            U[:, b:b + n, :], ALU.add).then_inc(looped, 1)
                    dve.wait_ge(looped, k * NQ + q + 1)
                    last = nc.vector.tensor_tensor(U[:, b:b + n, :], S1[q % 2][:, 0:n, :],
                                                   dinv2[:, b:b + n].unsqueeze(2).to_broadcast([P, n, D]), ALU.mult)
                    if q == NQ - 1:
                        last.then_inc(u_ready, 1)

            in_hops(dve, hop)
            dve.wait_ge(s1_added, HOPS * NQ)
            dve.wait_ge(u_ready, HOPS + 1)
            nc.vector.tensor_tensor(U[:], feats[:], dinv[:].unsqueeze(2).to_broadcast([P, NB, D]),
                                    ALU.mult).then_inc(final, 1)
            dve.wait_ge(final, 1)
            nc.vector.tensor_scalar(U[:], U[:], (1.0 - ALPHA) / HOPS, None, ALU.mult).then_inc(final, 1)
            dve.wait_ge(final, 2)
            nc.vector.scalar_tensor_tensor(out=feats[:], in0=x_res[:], scalar=ALPHA, in1=U[:],
                                           op0=ALU.mult, op1=ALU.add).then_inc(final, 1)
            dve.wait_ge(final, 3)


def node_layer(nc, tag, NB, N, ident, x_res, feats, weight, bias, out, a, q_out):
    with ExitStack() as ctx:
        def sb(name, shape, dt=F32):
            return ctx.enter_context(nc.sbuf_tensor(f"{tag}_{name}", shape, dt))

        def pair(name, shape):
            return [sb(f"{name}{s}", shape) for s in range(2)]

        def ps(name):
            return ctx.enter_context(nc.psum_tensor(f"{tag}_{name}", [P, 512], F32))

        def sem(name):
            return ctx.enter_context(nc.semaphore(f"{tag}_{name}"))

        with_q = q_out is not None
        w = sb("w", [D, D])
        eps = sb("eps", [P, 1])
        stage = pair("stage", [P, D])
        f_t = pair("f_t", [D, P])
        z = pair("z", [P, D])
        stats = pair("stats", [P, 6])
        mv = pair("mv", [P, 2])
        sd = pair("sd", [P, 1])
        rs = pair("rs", [P, 1])
        normed = pair("normed", [P, D])
        pause = sb("pause", [1, 1])
        tps = [ps("tps0"), ps("tps1")]
        yps = [ps("yps0"), ps("yps1")]
        if bias is not None:
            bias_row = sb("bias_row", [P, D])
        if with_q:
            x_t = pair("x_t", [D, P])
            wq_t = sb("wq_t", [DQ, D])
            wdot = sb("wdot", [DQ, DQ])
            wqd = sb("wqd", [D, DQ])
            q_all = sb("q_all", [P, NB, DQ])
            tqs = [ps("tqs0"), ps("tqs1")]
            qps = [ps("qps0"), ps("qps1")]

        w_in = sem("w_in")
        const = sem("const")
        biased = sem("biased")
        staged = sem("staged")
        f_turned = sem("f_turned")
        f_copied = sem("f_copied")
        multiplied = sem("multiplied")
        summed = sem("summed")
        steps = sem("steps")
        aggregated = sem("aggregated")
        rooted = sem("rooted")
        inverted = sem("inverted")
        normalised = sem("normalised")
        kept = sem("kept")
        x_turned = sem("x_turned")
        x_copied = sem("x_copied")
        q_done = sem("q_done")
        q_kept = sem("q_kept")
        stored = sem("stored")
        block = ctx.enter_context(nc.Block())

        def over_blocks(eng, step):
            for b in range(min(2, NB)):
                step(b, b)
            if NB >= 4:
                with eng.Fori(1, NB // 2) as k:
                    step(k * 2, 0)
                    step(k * 2 + 1, 1)
            if NB % 2 and NB > 2:
                step(NB - 1, 0)

        def later(b):
            return not isinstance(b, int) or b >= 2

        n_w = 16 * (1 + (bias is not None) + (1 + H) * with_q)

        @block.sync
        def _(sp):
            sp.dma_start(w[:], weight).then_inc(w_in, 16)
            if bias is not None:
                sp.dma_start(bias_row[:], bias.to_broadcast([P, D])).then_inc(w_in, 16)
            if with_q:
                sp.dma_start(wq_t[:], a["wq_t"]).then_inc(w_in, 16)
                sp.wait_ge(const, 2)
                for h in range(H):
                    e = DQ // H
                    sp.dma_start(wdot[h * e:(h + 1) * e, h * e:(h + 1) * e], a["Wdot"]).then_inc(w_in, 16)
            sp.wait_ge(kept, NB)
            whole, rest = divmod(N, P)
            if with_q:
                sp.dma_start(out, x_res[:]).then_inc(stored, 16)
                sp.wait_ge(q_kept, NB)
                sp.dma_start(q_out, q_all[:]).then_inc(stored, 16)
                sp.wait_ge(stored, 32)
            else:
                sp.dma_start(out[0:whole * P, :].rearrange("(b p) d -> p b d", p=P),
                             x_res[:, 0:whole, :]).then_inc(stored, 16)
                if rest:
                    sp.dma_start(out[whole * P:N, :], x_res[0:rest, whole, :]).then_inc(stored, 16)
                sp.wait_ge(stored, 16 + 16 * (rest > 0))

        @block.gpsimd
        def _(pool):
            nc.gpsimd.memset(eps[:], EPS).then_inc(const, 1)
            if with_q:
                nc.gpsimd.memset(wdot[:], 0.0).then_inc(const, 1)

            def step(b, s):
                if later(b):
                    pool.wait_ge(f_turned, b - 1)
                nc.gpsimd.tensor_copy(stage[s][:], feats[:, bass.ds(b, 1), :].rearrange("p o d -> p (o d)")
                                      ).then_inc(staged, 1)

            over_blocks(pool, step)

        @block.tensor
        def _(pe):
            pe.wait_ge(w_in, n_w)
            if with_q:
                nc.tensor.matmul(qps[1][:, 0:DQ], wq_t[:], wdot[:], start=True, stop=True).then_inc(q_done, 1)
            extra = 1 if with_q else 0

            def step(b, s):
                pe.wait_ge(staged, b + 1)
                if later(b):
                    pe.wait_ge(f_copied, b - 1)
                nc.tensor.transpose(tps[s][:, 0:P], stage[s][:], ident[:]).then_inc(f_turned, 1)
                pe.wait_ge(f_copied, b + 1)
                if later(b):
                    pe.wait_ge(summed, b - 1)
                nc.tensor.matmul(yps[s][:, 0:D], f_t[s][:], w[:], start=True, stop=True).then_inc(multiplied, 1)

            def queries(b, s):
                pe.wait_ge(normalised, b + 1)
                if later(b):
                    pe.wait_ge(x_copied, b - 1)
                nc.tensor.transpose(tqs[s][:, 0:P], normed[s][:], ident[:]).then_inc(x_turned, 1)
                pe.wait_ge(x_copied, b + 1)
                pe.wait_ge(q_kept, b - 1) if later(b) else pe.wait_ge(const, 3)
                nc.tensor.matmul(qps[s][:, 0:DQ], x_t[s][:], wqd[:], start=True, stop=True).then_inc(q_done, 1)

            def both(b, s):
                step(b, s)
                if with_q:
                    queries(b, s)

            over_blocks(pe, both)

        @block.scalar
        def _(act):
            act.wait_ge(const, 1)
            if with_q:
                act.wait_ge(q_done, 1)
                nc.scalar.copy(wqd[:], qps[1][:, 0:DQ]).then_inc(const, 1)

            def step(b, s):
                act.wait_ge(f_turned, b + 1)
                if later(b):
                    act.wait_ge(multiplied, b - 1)
                nc.scalar.copy(f_t[s][:], tps[s][:, 0:P]).then_inc(f_copied, 1)
                act.wait_ge(aggregated, b + 1)
                nc.scalar.activation(sd[s][:], mv[s][:, 1:2], ACT.Sqrt, bias=eps[:, 0:1]).then_inc(rooted, 1)
                if with_q:
                    act.wait_ge(x_turned, b + 1)
                    if later(b):
                        act.wait_ge(q_done, b)
                    nc.scalar.copy(x_t[s][:], tqs[s][:, 0:P]).then_inc(x_copied, 1)
                    act.wait_ge(q_done, b + 2)
                    nc.scalar.copy(q_all[:, bass.ds(b, 1), :].rearrange("p o d -> p (o d)"),
                                   qps[s][:, 0:DQ]).then_inc(q_kept, 1)

            over_blocks(act, step)

        @block.vector
        def _(dve):
            if bias is not None:
                dve.wait_ge(w_in, 32)
                dve.wait_ge(w_in, n_w)
                nc.vector.tensor_tensor(x_res[:], x_res[:],
                                        bias_row[:].unsqueeze(1).to_broadcast([P, NB, D]),
                                        ALU.add).then_inc(biased, 1)
                dve.wait_ge(biased, 1)

            def step(b, s):
                block_b = x_res[:, bass.ds(b, 1), :].rearrange("p o d -> p (o d)")
                dve.wait_ge(multiplied, b + 1)
                nc.vector.tensor_tensor(z[s][:], yps[s][:, 0:D], block_b, ALU.add).then_inc(summed, 1)
                dve.wait_ge(summed, b + 1)
                nc.vector.bn_stats(stats[s][:], z[s][:]).then_inc(steps, 1)
                dve.wait_ge(steps, b + 1)
                if later(b):
                    dve.wait_ge(normalised, b - 1)
                nc.vector.memset(pause[:], 0.0)
                nc.vector.bn_aggr(mv[s][:], stats[s][:]).then_inc(aggregated, 1)
                dve.wait_ge(rooted, b + 1)
                nc.vector.reciprocal(rs[s][:], sd[s][:]).then_inc(inverted, 1)
                dve.wait_ge(inverted, b + 1)
                if with_q and later(b):
                    dve.wait_ge(x_turned, b - 1)
                nc.vector.tensor_scalar(normed[s][:], z[s][:], mv[s][:, 0:1], rs[s][:, 0:1],
                                        ALU.subtract, ALU.mult).then_inc(normalised, 1)
                nc.vector.tensor_scalar(block_b, z[s][:], mv[s][:, 0:1], rs[s][:, 0:1],
                                        ALU.subtract, ALU.mult).then_inc(kept, 1)

            over_blocks(dve, step)
            dve.wait_ge(kept, NB)


def edge_attention(nc, a, x1_table, q_table, sums_table, ident, G):
    with ExitStack() as ctx:
        def sb(name, shape, dt=F32):
            return ctx.enter_context(nc.sbuf_tensor(f"e_{name}", shape, dt))

        def pair(name, shape, dt=F32):
            return [sb(f"{name}{s}", shape, dt) for s in range(2)]

        def bank(name):
            return ctx.enter_context(nc.psum_tensor(f"e_{name}", [P, GE], F32))

        def sem(name):
            return ctx.enter_context(nc.semaphore(f"e_{name}"))

        wang_k = sb("wang_k", [EA, D])
        wang_v = sb("wang_v", [EA, D])
        wlin_k = sb("wlin_k", [D, DQ])
        wlin_v = sb("wlin_v", [D, D])
        w1 = sb("w1", [EA, 2 * HID])
        b1 = sb("b1", [2 * HID, 1])
        w2k = sb("w2k", [2 * HID, DQ])
        w2v = sb("w2v", [2 * HID, D])
        head_sum = sb("head_sum", [DQ, D])
        head_pick = sb("head_pick", [D, H])
        ones = sb("ones", [P, P])
        pause = sb("pause", [1, 1])
        src_ix = pair("src_ix", [P, GT], I32)
        dst_ix = pair("dst_ix", [P, GT], I32)
        x_rows = pair("x_rows", [P, GT, D])
        q_rows = pair("q_rows", [P, GT, DQ])
        sh_t = pair("sh_t", [EA, GE])
        ea_t = pair("ea_t", [EA, GE])
        dst_now = pair("dst_now", [P, GE], I32)
        dst_old = pair("dst_old", [P, GE], I32)
        x_t = pair("x_t", [D, GE])
        q_t = pair("q_t", [DQ, GE])
        hidden = pair("hidden", [2 * HID, GE])
        x_gk = pair("x_gk", [D, GE])
        x_gv = pair("x_gv", [D, GE])
        rad_k = pair("rad_k", [DQ, GE])
        rad_v = pair("rad_v", [D, GE])
        key = pair("key", [DQ, GE])
        prod = pair("prod", [DQ, GE])
        value = pair("value", [D, GE])
        fresh = pair("fresh", [P, GE])
        top = pair("top", [P, GE + 1])
        drop = pair("drop", [P, GE])
        lift = pair("lift", [P, GE])
        weight = pair("weight", [P, GE])
        decay = pair("decay", [P, GE])
        weighted = pair("weighted", [P, GE])
        wsum = pair("wsum", [P, GE])
        vsum = pair("vsum", [P, GE])
        out_rows = pair("out_rows", [P, GT, ROW])

        b_x = bank("b_x")
        b_gk = bank("b_gk")
        b_gv = bank("b_gv")
        b_r = bank("b_r")
        b_lk = bank("b_lk")
        b_lv = bank("b_lv")
        b_rk = bank("b_rk")
        b_o = bank("b_o")

        w_in = sem("w_in")
        const = sem("const")
        paused = sem("paused")
        ix_in = [sem("ix_in0"), sem("ix_in1")]
        feat_in = [sem("feat_in0"), sem("feat_in1")]
        dst_in = [sem("dst_in0"), sem("dst_in1")]
        x_got = [sem("x_got0"), sem("x_got1")]
        q_got = [sem("q_got0"), sem("q_got1")]
        p_x = sem("p_x")
        p_q = sem("p_q")
        p_gk = sem("p_gk")
        p_gv = sem("p_gv")
        p_hid = sem("p_hid")
        p_lk = sem("p_lk")
        p_lv = sem("p_lv")
        p_rk = sem("p_rk")
        p_rv = sem("p_rv")
        p_score = sem("p_score")
        p_out = sem("p_out")
        a_x = sem("a_x")
        a_q = sem("a_q")
        a_hid = sem("a_hid")
        a_rk = sem("a_rk")
        a_rv = sem("a_rv")
        a_weight = sem("a_weight")
        a_decay = sem("a_decay")
        a_sums = sem("a_sums")
        a_dens = sem("a_dens")
        v_gk = sem("v_gk")
        v_gv = sem("v_gv")
        v_key = sem("v_key")
        v_prod = sem("v_prod")
        v_value = sem("v_value")
        v_step = sem("v_step")
        v_fresh = sem("v_fresh")
        v_top = sem("v_top")
        v_drop = sem("v_drop")
        v_lift = sem("v_lift")
        v_half = sem("v_half")
        v_weighted = sem("v_weighted")
        v_wsum = sem("v_wsum")
        v_vsum = sem("v_vsum")
        stored = [sem("stored0"), sem("stored1")]
        block = ctx.enter_context(nc.Block())

        n_w = 16 * 8

        def slots(i, s):
            return (i // 2 + 1) * 16 if isinstance(i, int) else None

        def each_group(eng, step, lag):
            last = G + lag
            peeled = 2 + lag + (lag % 2)
            for i in range(peeled):
                step(i, i % 2, i // 2)
            n_pairs = (G - peeled) // 2
            if n_pairs > 0:
                with eng.Fori(peeled // 2, peeled // 2 + n_pairs) as k:
                    step(k * 2, 0, k)
                    step(k * 2 + 1, 1, k)
            for i in range(peeled + 2 * n_pairs, last):
                step(i, i % 2, i // 2)

        def on(i, lag):
            return not isinstance(i, int) or 0 <= i - lag < G

        def used(i, lag=0):
            return not isinstance(i, int) or i - lag >= 2

        def prior(i, lag=0):
            return not isinstance(i, int) or i - lag >= 1

        @block.sync
        def _(sp):
            for dst, name in ((wang_k, "wang_k_t"), (wang_v, "wang_v_t"), (wlin_k, "Wlin_k"),
                              (wlin_v, "Wlin_v"), (w1, "W1"), (b1, "b1")):
                sp.dma_start(dst[:], a[name]).then_inc(w_in, 16)
            sp.wait_ge(const, 2)
            sp.dma_start(w2k[0:HID, :], a["W2k"]).then_inc(w_in, 16)
            sp.dma_start(w2v[HID:2 * HID, :], a["W2v"]).then_inc(w_in, 16)

            def step(i, s, k):
                cols = bass.ds(i * GE, GE)
                if used(i):
                    sp.wait_ge(x_got[s], k * 64)
                    sp.wait_ge(q_got[s], k * 64)
                tiles = bass.ds(i * GT, GT)
                sp.dma_start(src_ix[s][:], a["src_cols"][:, tiles]).then_inc(ix_in[s], 16)
                sp.dma_start(dst_ix[s][:], a["dst_cols"][:, tiles]).then_inc(ix_in[s], 16)
                if used(i):
                    sp.wait_ge(p_hid, i - 1)
                sp.dma_start(sh_t[s][:], a["sh_t"][:, cols]).then_inc(feat_in[s], 16)
                sp.dma_start(ea_t[s][:], a["ea_t"][:, cols]).then_inc(feat_in[s], 16)
                if used(i):
                    sp.wait_ge(v_step, i - 1)
                sp.dma_start(dst_now[s][:], a["dst"][:, cols].to_broadcast([P, GE])).then_inc(dst_in[s], 16)
                sp.dma_start(dst_old[s][:], a["dst_before"][:, cols].to_broadcast([P, GE])).then_inc(dst_in[s], 16)

            each_group(sp, step, 0)

        @block.gpsimd
        def _(pool):
            nc.gpsimd.memset(w2k[:], 0.0).then_inc(const, 1)
            nc.gpsimd.memset(w2v[:], 0.0).then_inc(const, 1)
            nc.gpsimd.memset(ones[:], 1.0).then_inc(const, 1)
            nc.gpsimd.memset(top[1][:, GE:GE + 1], 0.0).then_inc(const, 1)
            nc.gpsimd.memset(wsum[1][:, GE - 1:GE], 0.0).then_inc(const, 1)
            nc.gpsimd.memset(vsum[1][:, GE - 1:GE], 0.0).then_inc(const, 1)
            nc.gpsimd.memset(pause[:], 0.0).then_inc(const, 1)
            pool.wait_ge(const, 7)
            per_q, per_v = DQ // H, D // H
            hs = head_sum[:].rearrange("k (h c) -> k h c", c=per_v)
            nc.gpsimd.affine_select(out=hs, in_=ones[0:DQ, :].rearrange("k (h c) -> k h c", c=per_v),
                                    compare_op=ALU.is_ge, fill=0.0, base=0,
                                    pattern=[[-per_q, H], [0, per_v]], channel_multiplier=1).then_inc(const, 1)
            pool.wait_ge(const, 8)
            nc.gpsimd.affine_select(out=hs, in_=hs, compare_op=ALU.is_ge, fill=0.0, base=per_q - 1,
                                    pattern=[[per_q, H], [0, per_v]], channel_multiplier=-1).then_inc(const, 1)
            nc.gpsimd.affine_select(out=head_pick[:], in_=ones[:, 0:H], compare_op=ALU.is_equal, fill=0.0, base=0,
                                    pattern=[[-per_v, H]], channel_multiplier=1).then_inc(const, 1)

            def step(i, s, k):
                pool.wait_ge(ix_in[s], k * 32 + 32)
                if used(i):
                    pool.wait_ge(p_x, i - 1)
                    pool.wait_ge(p_q, i - 1)
                if prior(i):
                    pool.wait_ge(paused, i)
                nc.gpsimd.tensor_tensor(pause[:], pause[:], pause[:], ALU.add).then_inc(paused, 1)
                for j in range(GT):
                    nc.gpsimd.indirect_dma_start(
                        x_rows[s][:, j, :], None, x1_table,
                        bass.IndirectOffsetOnAxis(ap=src_ix[s][:, j:j + 1], axis=0)).then_inc(x_got[s], 16)
                for j in range(GT):
                    nc.gpsimd.indirect_dma_start(
                        q_rows[s][:, j, :], None, q_table,
                        bass.IndirectOffsetOnAxis(ap=dst_ix[s][:, j:j + 1], axis=0)).then_inc(q_got[s], 16)

            each_group(pool, step, 0)

        @block.tensor
        def _(pe):
            pe.wait_ge(w_in, n_w)
            pe.wait_ge(const, 10)

            def step(i, s, k):
                o = 1 - s
                if on(i, 1):
                    pe.wait_ge(v_gk, i)
                    if prior(i, 1):
                        pe.wait_ge(v_key, i - 1)
                    nc.tensor.matmul(b_lk[0:DQ, :], wlin_k[:], x_gk[o][:], start=True, stop=True).then_inc(p_lk, 1)
                    pe.wait_ge(a_hid, i)
                    if prior(i, 1):
                        pe.wait_ge(a_rk, i - 1)
                    nc.tensor.matmul(b_rk[0:DQ, :], w2k[:], hidden[o][:], start=True, stop=True).then_inc(p_rk, 1)
                    nc.tensor.matmul(b_r[:], w2v[:], hidden[o][:], start=True, stop=True).then_inc(p_rv, 1)
                    pe.wait_ge(v_gv, i)
                    if prior(i, 1):
                        pe.wait_ge(v_value, i - 1)
                    nc.tensor.matmul(b_lv[:], wlin_v[:], x_gv[o][:], start=True, stop=True).then_inc(p_lv, 1)
                if on(i, 0):
                    if prior(i):
                        pe.wait_ge(a_q, i)
                    pe.wait_ge(x_got[s], k * 64 + 64)
                    for j in range(GT):
                        tr = nc.tensor.transpose(b_x[:, j * P:(j + 1) * P], x_rows[s][:, j, :], ident[:])
                    tr.then_inc(p_x, 1)
                    pe.wait_ge(feat_in[s], k * 32 + 32)
                    if prior(i, 1):
                        pe.wait_ge(a_dens, i - 2) if (not isinstance(i, int) or i - 2 > 0) else None
                    nc.tensor.matmul(b_gk[:], wang_k[:], sh_t[s][:], start=True, stop=True).then_inc(p_gk, 1)
                    if prior(i, 1):
                        pe.wait_ge(v_drop, i - 1)
                    nc.tensor.matmul(b_gv[:], wang_v[:], sh_t[s][:], start=True, stop=True).then_inc(p_gv, 1)
                    if prior(i):
                        pe.wait_ge(a_rv, i)
                    pe.wait_ge(a_x, i + 1)
                    pe.wait_ge(q_got[s], k * 64 + 64)
                    nc.tensor.matmul(b_r[:], w1[:], ea_t[s][:], start=True, stop=True).then_inc(p_hid, 1)
                    for j in range(GT):
                        tr = nc.tensor.transpose(b_x[0:DQ, j * P:(j + 1) * P], q_rows[s][:, j, :], ident[:])
                    tr.then_inc(p_q, 1)
                if on(i, 1):
                    pe.wait_ge(v_prod, i)
                    if on(i, 0):
                        pe.wait_ge(v_gv, i + 1)
                    else:
                        pe.wait_ge(v_drop, i - 1)
                    nc.tensor.matmul(b_gv[:], head_sum[:], prod[o][:], start=True, stop=True).then_inc(p_score, 1)
                if on(i, 2):
                    pe.wait_ge(v_vsum, i - 1)
                    if prior(i, 2):
                        pe.wait_ge(a_sums, i - 2)
                        pe.wait_ge(a_dens, i - 2)
                    if on(i, 0):
                        pe.wait_ge(v_gk, i + 1)
                    for j in range(GT):
                        nc.tensor.transpose(b_o[:, j * P:(j + 1) * P], vsum[s][:, j * P:(j + 1) * P], ident[:])
                    for j in range(GT):
                        mm = nc.tensor.matmul(b_gk[:, j * H:(j + 1) * H], wsum[s][:, j * P:(j + 1) * P],
                                              head_pick[:], start=True, stop=True)
                    mm.then_inc(p_out, 1)

            each_group(pe, step, 2)

        @block.scalar
        def _(act):
            act.wait_ge(w_in, n_w)

            def step(i, s, k):
                o = 1 - s
                if on(i, 1):
                    act.wait_ge(p_rk, i)
                    if used(i, 1):
                        act.wait_ge(v_key, i - 2)
                    nc.scalar.copy(rad_k[o][:], b_rk[0:DQ, :]).then_inc(a_rk, 1)
                    act.wait_ge(p_rv, i)
                    if used(i, 1):
                        act.wait_ge(v_value, i - 2)
                    nc.scalar.copy(rad_v[o][:], b_r[:]).then_inc(a_rv, 1)
                if on(i, 0):
                    act.wait_ge(p_x, i + 1)
                    if used(i):
                        act.wait_ge(v_gv, i - 1)
                    nc.scalar.copy(x_t[s][:], b_x[:]).then_inc(a_x, 1)
                    act.wait_ge(p_hid, i + 1)
                    if used(i):
                        act.wait_ge(p_rv, i - 1)
                    nc.scalar.activation(hidden[s][:], b_r[:], ACT.Relu, bias=b1[:, 0:1]).then_inc(a_hid, 1)
                    act.wait_ge(p_q, i + 1)
                    if used(i):
                        act.wait_ge(v_prod, i - 1)
                    nc.scalar.copy(q_t[s][:], b_x[0:DQ, :]).then_inc(a_q, 1)
                if on(i, 2):
                    act.wait_ge(p_out, i - 1)
                    if used(i, 2):
                        act.wait_ge(stored[s], 16 * k - 16)
                    nc.scalar.copy(out_rows[s][:, :, 0:D],
                                   b_o[:].rearrange("p (j d) -> p j d", d=D)).then_inc(a_sums, 1)
                    nc.scalar.copy(out_rows[s][:, :, D:ROW],
                                   b_gk[:, 0:GT * H].rearrange("p (j h) -> p j h", h=H)).then_inc(a_dens, 1)
                    act.wait_ge(a_dens, i - 1)
                    act.dma_start(sums_table[bass.ds((i - 2) * GE, GE), :].rearrange("(j p) r -> p j r", p=P),
                                  out_rows[s][:]).then_inc(stored[s], 16)
                if on(i, 1):
                    act.wait_ge(v_drop, i)
                    if used(i, 1):
                        act.wait_ge(v_wsum, i - 2)
                    nc.scalar.activation(weight[o][:], drop[o][:], ACT.Exp).then_inc(a_weight, 1)
                    act.wait_ge(v_lift, i)
                    if used(i, 1):
                        act.wait_ge(v_vsum, i - 2)
                    nc.scalar.activation(decay[o][:], lift[o][:], ACT.Exp).then_inc(a_decay, 1)

            each_group(act, step, 2)
            act.wait_ge(stored[0], 16 * (G // 2))
            act.wait_ge(stored[1], 16 * (G // 2))

        @block.vector
        def _(dve):
            dve.wait_ge(const, 7)

            def step(i, s, k):
                o = 1 - s
                if on(i, 1):
                    dve.wait_ge(p_lk, i)
                    dve.wait_ge(a_rk, i)
                    nc.vector.tensor_tensor(key[o][:], b_lk[0:DQ, :], rad_k[o][:], ALU.mult).then_inc(v_key, 1)
                if on(i, 0):
                    dve.wait_ge(p_gk, i + 1)
                    dve.wait_ge(a_x, i + 1)
                    if used(i):
                        dve.wait_ge(p_lk, i - 1)
                    nc.vector.tensor_tensor(x_gk[s][:], b_gk[:], x_t[s][:], ALU.mult).then_inc(v_gk, 1)
                if on(i, 1):
                    dve.wait_ge(v_key, i)
                    dve.wait_ge(a_q, i)
                    if used(i, 1):
                        dve.wait_ge(p_score, i - 2)
                    nc.vector.tensor_tensor(prod[o][:], key[o][:], q_t[o][:], ALU.mult).then_inc(v_prod, 1)
                if on(i, 0):
                    dve.wait_ge(p_gv, i + 1)
                    if used(i):
                        dve.wait_ge(p_lv, i - 1)
                    nc.vector.tensor_tensor(x_gv[s][:], b_gv[:], x_t[s][:], ALU.mult).then_inc(v_gv, 1)
                if on(i, 1):
                    dve.wait_ge(p_lv, i)
                    dve.wait_ge(a_rv, i)
                    if used(i, 1):
                        dve.wait_ge(v_weighted, i - 2)
                    nc.vector.tensor_tensor(value[o][:], b_lv[:], rad_v[o][:], ALU.mult).then_inc(v_value, 1)
                if on(i, 0):
                    dve.wait_ge(dst_in[s], k * 32 + 32)
                    if used(i):
                        dve.wait_ge(v_lift, i - 1)
                    nc.vector.tensor_tensor(fresh[s][:], dst_now[s][:], dst_old[s][:], ALU.not_equal).then_inc(v_step, 1)
                if on(i, 2):
                    dve.wait_ge(a_weight, i - 1)
                    if used(i, 2):
                        dve.wait_ge(v_vsum, i - 3)
                    nc.vector.tensor_tensor(weighted[s][:], weight[s][:], value[s][:], ALU.mult).then_inc(v_weighted, 1)
                    dve.wait_ge(a_decay, i - 1)
                    if used(i, 2):
                        dve.wait_ge(p_out, i - 3)
                    if prior(i, 2):
                        dve.wait_ge(v_wsum, i - 2)
                    nc.vector.tensor_tensor_scan(out=wsum[s][:], data0=decay[s][:], data1=weight[s][:],
                                                 initial=wsum[o][:, GE - 1:GE], op0=ALU.mult,
                                                 op1=ALU.add).then_inc(v_wsum, 1)
                if on(i, 0):
                    dve.wait_ge(v_step, i + 1)
                    nc.vector.tensor_scalar(fresh[s][:], fresh[s][:], -BIG, None, ALU.mult).then_inc(v_fresh, 1)
                if on(i, 2):
                    dve.wait_ge(v_weighted, i - 1)
                    if prior(i, 2):
                        dve.wait_ge(v_vsum, i - 2)
                    nc.vector.tensor_tensor_scan(out=vsum[s][:], data0=decay[s][:], data1=weighted[s][:],
                                                 initial=vsum[o][:, GE - 1:GE], op0=ALU.mult,
                                                 op1=ALU.add).then_inc(v_vsum, 1)
                if on(i, 1):
                    dve.wait_ge(v_fresh, i)
                    dve.wait_ge(p_score, i)
                    if prior(i, 1):
                        dve.wait_ge(v_lift, i - 1)
                    nc.vector.tensor_copy(top[o][:, 0:1], top[s][:, GE:GE + 1])
                    nc.vector.tensor_tensor_scan(out=top[o][:, 1:GE + 1], data0=fresh[o][:], data1=b_gv[:],
                                                 initial=top[s][:, GE:GE + 1], op0=ALU.add,
                                                 op1=ALU.max).then_inc(v_top, 1)
                    dve.wait_ge(v_top, i)
                    if used(i, 1):
                        dve.wait_ge(a_weight, i - 2)
                        dve.wait_ge(a_decay, i - 2)
                    nc.vector.tensor_tensor(lift[o][:], fresh[o][:], top[o][:, 1:GE + 1], ALU.subtract).then_inc(v_half, 1)
                    nc.vector.tensor_tensor(drop[o][:], b_gv[:], top[o][:, 1:GE + 1], ALU.subtract).then_inc(v_drop, 1)
                    dve.wait_ge(v_half, i)
                    nc.vector.tensor_tensor(lift[o][:], lift[o][:], top[o][:, 0:GE], ALU.add).then_inc(v_lift, 1)

            each_group(dve, step, 2)


def attention_output(nc, sums_table, last_edge, has_edges, feats, NB):
    with (nc.sbuf_tensor("last_rows", [P, NB, ROW], F32) as rows,
          nc.sbuf_tensor("inverse", [P, NB, H], F32) as inverse,
          nc.sbuf_tensor("inverse_kept", [P, NB, H], F32) as kept,
          nc.semaphore("rows_got") as rows_got,
          nc.semaphore("divided") as divided,
          nc.Block() as block):

        @block.gpsimd
        def _(pool):
            for b in range(NB):
                nc.gpsimd.indirect_dma_start(
                    rows[:, b, :], None, sums_table,
                    bass.IndirectOffsetOnAxis(ap=last_edge[:, b:b + 1], axis=0)).then_inc(rows_got, 16)

        @block.vector
        def _(dve):
            dve.wait_ge(rows_got, 16 * NB)
            nc.vector.reciprocal(inverse[:], rows[:, :, D:ROW]).then_inc(divided, 1)
            dve.wait_ge(divided, 1)
            nc.vector.tensor_tensor(kept[:], inverse[:], has_edges[:].unsqueeze(2).to_broadcast([P, NB, H]),
                                    ALU.mult).then_inc(divided, 1)
            dve.wait_ge(divided, 2)
            nc.vector.tensor_tensor(feats[:].rearrange("p b (h c) -> p b h c", h=H),
                                    rows[:, :, 0:D].rearrange("p b (h c) -> p b h c", h=H),
                                    kept[:].unsqueeze(3).to_broadcast([P, NB, H, D // H]),
                                    ALU.mult).then_inc(divided, 1)
            dve.wait_ge(divided, 3)


_OUT = ((6250, 128), "float32")


def kernel(**inputs):
    import concourse.bacc as _bacc
    from concourse import mybir as _mybir
    from concourse.bass_utils import run_bass_kernel_spmd as _run

    n_nodes, n_edges = inputs["x"].shape[0], inputs["src"].shape[0]
    np_rows = (n_nodes // P + 1) * P
    padded = -(-n_edges // (2 * GE)) * 2 * GE

    def rows(v, n):
        return np.concatenate([v, np.zeros((n - v.shape[0],) + v.shape[1:], v.dtype)])

    fill = np.full(padded - n_edges, n_nodes, np.int32)
    src = np.concatenate([np.asarray(inputs["src"], np.int32), fill])
    dst = np.concatenate([np.asarray(inputs["dst"], np.int32), fill])
    v = {k: np.asarray(x) for k, x in inputs.items()}
    arrays = {
        "x": rows(v["x"], np_rows),
        "src": src[None, :], "dst": dst[None, :],
        "dst_before": np.concatenate([np.full(1, -1, np.int32), dst[:-1]])[None, :],
        "src_cols": src.reshape(-1, P).T, "dst_cols": dst.reshape(-1, P).T,
        "ea_t": rows(v["edge_attr_16"], padded).T, "sh_t": rows(v["edge_attr_16_n2"], padded).T,
        "w0_t": v["L0_gnn_weight"].T, "b0": v["L0_gnn_bias"][None, :],
        "wq_t": v["L1_gnn_Wq"].T, "Wdot": v["L1_gnn_Wdot"], "Wout": v["L1_gnn_Wout"],
        "wang_k_t": v["L1_gnn_Wang_k"].T, "wang_v_t": v["L1_gnn_Wang_v"].T,
        "Wlin_k": v["L1_gnn_Wlin_k"], "Wlin_v": v["L1_gnn_Wlin_v"],
        "W1": np.concatenate([v["L1_gnn_W1k"], v["L1_gnn_W1v"]], axis=1),
        "b1": np.concatenate([v["L1_gnn_b1k"], v["L1_gnn_b1v"]])[:, None],
        "W2k": v["L1_gnn_W2k"], "W2v": v["L1_gnn_W2v"],
    }
    arrays = {k: np.ascontiguousarray(x) for k, x in arrays.items()}
    nc = _bacc.Bacc("TRN2", target_bir_lowering=False, num_devices=1)
    a = {k: nc.dram_tensor(f"in_{k}", x.shape, _mybir.dt.from_np(x.dtype), kind="ExternalInput").ap()
         for k, x in arrays.items()}
    a["n_nodes"] = n_nodes
    out = nc.dram_tensor("out", (n_nodes, D), F32, kind="ExternalOutput").ap()
    program(nc, a, out)
    r = _run(nc, [{f"in_{k}": x for k, x in arrays.items()}], core_ids=[0])
    return r.results[0]["out"]
```
